# Optimizing a Trainium2 kernel written in Bass

```python
import numpy as np
import jax
import jax.numpy as jnp

def _softmax(x, axis=-1):
    return jax.nn.softmax(x, axis=axis)

def _gelu(x):
    return jax.nn.gelu(x, approximate=True)

def _silu(x):
    return jax.nn.silu(x)

def _sigmoid(x):
    return jax.nn.sigmoid(x)

def _layernorm(x, axis=-1, eps=1e-05):
    m = jnp.mean(x, axis=axis, keepdims=True)
    v = jnp.var(x, axis=axis, keepdims=True)
    return (x - m) / jnp.sqrt(v + eps)

def _scatter_add(tgt, idx, src, axis=0):
    return tgt.at[idx].add(src)

def _segment_sum(src, seg, n):
    return jax.ops.segment_sum(src, seg, n)
kernel_name = 'mk_dlrm_tower_d1_rec_r8_ab68e7'

def setup_inputs(seed: int=0):
    np.random.seed(seed)
    _w = jnp.asarray

    def _rec_inputs():
        import jax
        import jax.numpy as jnp
        _tk = jax.random.key(seed)
        dense_ctx = jax.random.normal(jax.random.fold_in(_tk, 190), (2048, 16), jnp.float32)
        ids = jnp.stack([jax.random.randint(jax.random.fold_in(_tk, 200 + f), (2048,), 0, v, jnp.int32) for f, v in enumerate([1000, 125000, 12500, 125000, 12500, 12500, 1000, 12500, 1250, 125000, 1000, 125000, 1250, 1000, 125000, 1250, 12500, 1000, 125000, 1250, 12500, 125000, 12500, 125000, 1000, 1000, 1250, 125000, 1000, 12500, 125000, 125000, 125000, 125000, 12500, 12500, 12500, 12500, 1250])], axis=1)
        tbl_0 = 0.05 * jax.random.normal(jax.random.fold_in(_tk, 500 + 0), (1000, 16), jnp.float32)
        tbl_1 = 0.05 * jax.random.normal(jax.random.fold_in(_tk, 500 + 1), (125000, 16), jnp.float32)
        tbl_2 = 0.05 * jax.random.normal(jax.random.fold_in(_tk, 500 + 2), (12500, 16), jnp.float32)
        tbl_3 = 0.05 * jax.random.normal(jax.random.fold_in(_tk, 500 + 3), (125000, 16), jnp.float32)
        tbl_4 = 0.05 * jax.random.normal(jax.random.fold_in(_tk, 500 + 4), (12500, 16), jnp.float32)
        tbl_5 = 0.05 * jax.random.normal(jax.random.fold_in(_tk, 500 + 5), (12500, 16), jnp.float32)
        tbl_6 = 0.05 * jax.random.normal(jax.random.fold_in(_tk, 500 + 6), (1000, 16), jnp.float32)
        tbl_7 = 0.05 * jax.random.normal(jax.random.fold_in(_tk, 500 + 7), (12500, 16), jnp.float32)
        tbl_8 = 0.05 * jax.random.normal(jax.random.fold_in(_tk, 500 + 8), (1250, 16), jnp.float32)
        tbl_9 = 0.05 * jax.random.normal(jax.random.fold_in(_tk, 500 + 9), (125000, 16), jnp.float32)
        tbl_10 = 0.05 * jax.random.normal(jax.random.fold_in(_tk, 500 + 10), (1000, 16), jnp.float32)
        tbl_11 = 0.05 * jax.random.normal(jax.random.fold_in(_tk, 500 + 11), (125000, 16), jnp.float32)
        tbl_12 = 0.05 * jax.random.normal(jax.random.fold_in(_tk, 500 + 12), (1250, 16), jnp.float32)
        tbl_13 = 0.05 * jax.random.normal(jax.random.fold_in(_tk, 500 + 13), (1000, 16), jnp.float32)
        tbl_14 = 0.05 * jax.random.normal(jax.random.fold_in(_tk, 500 + 14), (125000, 16), jnp.float32)
        tbl_15 = 0.05 * jax.random.normal(jax.random.fold_in(_tk, 500 + 15), (1250, 16), jnp.float32)
        tbl_16 = 0.05 * jax.random.normal(jax.random.fold_in(_tk, 500 + 16), (12500, 16), jnp.float32)
        tbl_17 = 0.05 * jax.random.normal(jax.random.fold_in(_tk, 500 + 17), (1000, 16), jnp.float32)
        tbl_18 = 0.05 * jax.random.normal(jax.random.fold_in(_tk, 500 + 18), (125000, 16), jnp.float32)
        tbl_19 = 0.05 * jax.random.normal(jax.random.fold_in(_tk, 500 + 19), (1250, 16), jnp.float32)
        tbl_20 = 0.05 * jax.random.normal(jax.random.fold_in(_tk, 500 + 20), (12500, 16), jnp.float32)
        tbl_21 = 0.05 * jax.random.normal(jax.random.fold_in(_tk, 500 + 21), (125000, 16), jnp.float32)
        tbl_22 = 0.05 * jax.random.normal(jax.random.fold_in(_tk, 500 + 22), (12500, 16), jnp.float32)
        tbl_23 = 0.05 * jax.random.normal(jax.random.fold_in(_tk, 500 + 23), (125000, 16), jnp.float32)
        tbl_24 = 0.05 * jax.random.normal(jax.random.fold_in(_tk, 500 + 24), (1000, 16), jnp.float32)
        tbl_25 = 0.05 * jax.random.normal(jax.random.fold_in(_tk, 500 + 25), (1000, 16), jnp.float32)
        tbl_26 = 0.05 * jax.random.normal(jax.random.fold_in(_tk, 500 + 26), (1250, 16), jnp.float32)
        tbl_27 = 0.05 * jax.random.normal(jax.random.fold_in(_tk, 500 + 27), (125000, 16), jnp.float32)
        tbl_28 = 0.05 * jax.random.normal(jax.random.fold_in(_tk, 500 + 28), (1000, 16), jnp.float32)
        tbl_29 = 0.05 * jax.random.normal(jax.random.fold_in(_tk, 500 + 29), (12500, 16), jnp.float32)
        tbl_30 = 0.05 * jax.random.normal(jax.random.fold_in(_tk, 500 + 30), (125000, 16), jnp.float32)
        tbl_31 = 0.05 * jax.random.normal(jax.random.fold_in(_tk, 500 + 31), (125000, 16), jnp.float32)
        tbl_32 = 0.05 * jax.random.normal(jax.random.fold_in(_tk, 500 + 32), (125000, 16), jnp.float32)
        tbl_33 = 0.05 * jax.random.normal(jax.random.fold_in(_tk, 500 + 33), (125000, 16), jnp.float32)
        tbl_34 = 0.05 * jax.random.normal(jax.random.fold_in(_tk, 500 + 34), (12500, 16), jnp.float32)
        tbl_35 = 0.05 * jax.random.normal(jax.random.fold_in(_tk, 500 + 35), (12500, 16), jnp.float32)
        tbl_36 = 0.05 * jax.random.normal(jax.random.fold_in(_tk, 500 + 36), (12500, 16), jnp.float32)
        tbl_37 = 0.05 * jax.random.normal(jax.random.fold_in(_tk, 500 + 37), (12500, 16), jnp.float32)
        tbl_38 = 0.05 * jax.random.normal(jax.random.fold_in(_tk, 500 + 38), (1250, 16), jnp.float32)
        _rk = jax.random.fold_in(_tk, 7)
        W_top1 = 0.0606339 * jax.random.normal(jax.random.fold_in(_tk, 801), (272, 512), jnp.float32)
        W_top2 = 0.0441942 * jax.random.normal(jax.random.fold_in(_tk, 802), (512, 256), jnp.float32)
        W_top3 = 0.0625 * jax.random.normal(jax.random.fold_in(_tk, 803), (256, 1), jnp.float32)
        b_top1 = jnp.zeros((512,), jnp.float32)
        b_top2 = jnp.zeros((256,), jnp.float32)
        return (dense_ctx, ids, tbl_0, tbl_1, tbl_2, tbl_3, tbl_4, tbl_5, tbl_6, tbl_7, tbl_8, tbl_9, tbl_10, tbl_11, tbl_12, tbl_13, tbl_14, tbl_15, tbl_16, tbl_17, tbl_18, tbl_19, tbl_20, tbl_21, tbl_22, tbl_23, tbl_24, tbl_25, tbl_26, tbl_27, tbl_28, tbl_29, tbl_30, tbl_31, tbl_32, tbl_33, tbl_34, tbl_35, tbl_36, tbl_37, tbl_38, W_top1, b_top1, W_top2, b_top2, W_top3)
    dense_ctx, ids, tbl_0, tbl_1, tbl_2, tbl_3, tbl_4, tbl_5, tbl_6, tbl_7, tbl_8, tbl_9, tbl_10, tbl_11, tbl_12, tbl_13, tbl_14, tbl_15, tbl_16, tbl_17, tbl_18, tbl_19, tbl_20, tbl_21, tbl_22, tbl_23, tbl_24, tbl_25, tbl_26, tbl_27, tbl_28, tbl_29, tbl_30, tbl_31, tbl_32, tbl_33, tbl_34, tbl_35, tbl_36, tbl_37, tbl_38, W_top1, b_top1, W_top2, b_top2, W_top3 = _rec_inputs()

    def _L0_rec_setup():
        import jax, jax.numpy as jnp
        import numpy as np
        B, F0, D = (256, 39, 16)
        H1, H2 = (128, 128)
        key = jax.random.key(seed)
        k1, k2, k3 = jax.random.split(key, 3)
        x = jax.random.normal(k1, (B, F0, D), dtype=jnp.float32)

        def xavier(k, out_c, in_c):
            bound = np.sqrt(6.0 / (in_c + out_c)).astype(np.float32)
            return jax.random.uniform(k, (out_c, in_c, 1), dtype=jnp.float32, minval=-bound, maxval=bound)
        W0 = xavier(k2, H1, F0 * F0)
        W1 = xavier(k3, H2, F0 * H1)
        return {'input': x, 'W0': W0, 'W1': W1}
    _L0_rec_all = _L0_rec_setup()
    _L0_rec_in = {k: v for k, v in _L0_rec_all.items() if k in ('W0', 'W1')}
    del _L0_rec_all
    return {'dense_ctx': dense_ctx, 'ids': ids, 'tbl_0': tbl_0, 'tbl_1': tbl_1, 'tbl_2': tbl_2, 'tbl_3': tbl_3, 'tbl_4': tbl_4, 'tbl_5': tbl_5, 'tbl_6': tbl_6, 'tbl_7': tbl_7, 'tbl_8': tbl_8, 'tbl_9': tbl_9, 'tbl_10': tbl_10, 'tbl_11': tbl_11, 'tbl_12': tbl_12, 'tbl_13': tbl_13, 'tbl_14': tbl_14, 'tbl_15': tbl_15, 'tbl_16': tbl_16, 'tbl_17': tbl_17, 'tbl_18': tbl_18, 'tbl_19': tbl_19, 'tbl_20': tbl_20, 'tbl_21': tbl_21, 'tbl_22': tbl_22, 'tbl_23': tbl_23, 'tbl_24': tbl_24, 'tbl_25': tbl_25, 'tbl_26': tbl_26, 'tbl_27': tbl_27, 'tbl_28': tbl_28, 'tbl_29': tbl_29, 'tbl_30': tbl_30, 'tbl_31': tbl_31, 'tbl_32': tbl_32, 'tbl_33': tbl_33, 'tbl_34': tbl_34, 'tbl_35': tbl_35, 'tbl_36': tbl_36, 'tbl_37': tbl_37, 'tbl_38': tbl_38, 'W_top1': W_top1, 'b_top1': b_top1, 'W_top2': W_top2, 'b_top2': b_top2, 'W_top3': W_top3, 'L0_rec_W0': _L0_rec_in['W0'], 'L0_rec_W1': _L0_rec_in['W1']}

def reference(dense_ctx, ids, tbl_0, tbl_1, tbl_2, tbl_3, tbl_4, tbl_5, tbl_6, tbl_7, tbl_8, tbl_9, tbl_10, tbl_11, tbl_12, tbl_13, tbl_14, tbl_15, tbl_16, tbl_17, tbl_18, tbl_19, tbl_20, tbl_21, tbl_22, tbl_23, tbl_24, tbl_25, tbl_26, tbl_27, tbl_28, tbl_29, tbl_30, tbl_31, tbl_32, tbl_33, tbl_34, tbl_35, tbl_36, tbl_37, tbl_38, W_top1, b_top1, W_top2, b_top2, W_top3, L0_rec_W0, L0_rec_W1):
    import jax
    import jax.numpy as jnp

    def _L0_rec_ref(input, W0, W1):
        import jax, jax.numpy as jnp
        import numpy as np
        B, F0, D = (256, 39, 16)
        H1, H2 = (128, 128)
        x0 = input
        h = input
        outs = []
        for W in (W0, W1):
            Hout, P, _ = W.shape
            Hk = h.shape[1]
            Wr = W[:, :, 0].reshape(Hout, x0.shape[1], Hk)
            h = jnp.einsum('bfd,bqd,hfq->bhd', x0, h, Wr)
            outs.append(h)
        result = jnp.concatenate(outs, axis=1)
        return jnp.sum(result, axis=2)
    e = jnp.stack([tbl_0[ids[:, 0]], tbl_1[ids[:, 1]], tbl_2[ids[:, 2]], tbl_3[ids[:, 3]], tbl_4[ids[:, 4]], tbl_5[ids[:, 5]], tbl_6[ids[:, 6]], tbl_7[ids[:, 7]], tbl_8[ids[:, 8]], tbl_9[ids[:, 9]], tbl_10[ids[:, 10]], tbl_11[ids[:, 11]], tbl_12[ids[:, 12]], tbl_13[ids[:, 13]], tbl_14[ids[:, 14]], tbl_15[ids[:, 15]], tbl_16[ids[:, 16]], tbl_17[ids[:, 17]], tbl_18[ids[:, 18]], tbl_19[ids[:, 19]], tbl_20[ids[:, 20]], tbl_21[ids[:, 21]], tbl_22[ids[:, 22]], tbl_23[ids[:, 23]], tbl_24[ids[:, 24]], tbl_25[ids[:, 25]], tbl_26[ids[:, 26]], tbl_27[ids[:, 27]], tbl_28[ids[:, 28]], tbl_29[ids[:, 29]], tbl_30[ids[:, 30]], tbl_31[ids[:, 31]], tbl_32[ids[:, 32]], tbl_33[ids[:, 33]], tbl_34[ids[:, 34]], tbl_35[ids[:, 35]], tbl_36[ids[:, 36]], tbl_37[ids[:, 37]], tbl_38[ids[:, 38]]], axis=1)
    z = _L0_rec_ref(e, L0_rec_W0, L0_rec_W1)
    z = z.reshape(z.shape[0], -1)
    h = jnp.concatenate([z, dense_ctx], axis=1)
    h = jnp.maximum(h @ W_top1 + b_top1, 0.0)
    h = jnp.maximum(h @ W_top2 + b_top2, 0.0)
    y = h @ W_top3
    return y

_drawn_inputs = setup_inputs


def setup_inputs(seed=0):
    import zlib

    import numpy as np

    out = dict(_drawn_inputs(seed))
    spreads = {'b_top1': (0.0, 0.1), 'b_top2': (0.0, 0.1)}
    factors = {'tbl_0': 6.636,
     'tbl_1': 6.228,
     'tbl_2': 6.754,
     'tbl_3': 6.776,
     'tbl_4': 6.91,
     'tbl_5': 7.015,
     'tbl_6': 6.94,
     'tbl_7': 6.977,
     'tbl_8': 7.103,
     'tbl_9': 6.764,
     'tbl_10': 6.862,
     'tbl_11': 6.521,
     'tbl_12': 7.128,
     'tbl_13': 6.965,
     'tbl_14': 6.949,
     'tbl_15': 7.218,
     'tbl_16': 6.395,
     'tbl_17': 7.507,
     'tbl_18': 6.739,
     'tbl_19': 7.306,
     'tbl_20': 6.742,
     'tbl_21': 7.336,
     'tbl_22': 7.208,
     'tbl_23': 7.008,
     'tbl_24': 6.304,
     'tbl_25': 6.853,
     'tbl_26': 6.538,
     'tbl_27': 7.089,
     'tbl_28': 6.824,
     'tbl_29': 6.888,
     'tbl_30': 6.721,
     'tbl_31': 6.556,
     'tbl_32': 6.72,
     'tbl_33': 6.695,
     'tbl_34': 7.028,
     'tbl_35': 6.741,
     'tbl_36': 7.251,
     'tbl_37': 6.433,
     'tbl_38': 7.03,
     'L0_rec_W1': 8.0}
    for name, (base, spread) in spreads.items():
        noise = np.random.default_rng([zlib.crc32(name.encode()), seed]).standard_normal(out[name].shape)
        drawn = base * np.exp(spread * noise) if base else spread * noise
        out[name] = jnp.asarray(drawn.astype(out[name].dtype))
    for name, factor in factors.items():
        out[name] = (out[name] * factor).astype(out[name].dtype)
    return out
```

```python
import concourse.bass as bass
from concourse import mybir
from contextlib import ExitStack

B, F, D = 2048, 39, 16
H = 128
P = 128
F1 = F + 1
PARTS = 3
SH = 3
R = SH * F
NSHIFT = (F + 1) // 2
J = -(-NSHIFT // SH)
TILES = B // P
NB = 512
BPT = P * D // NB
CB = 2 * BPT
GB = 2 * P
GROUPS = B // GB
BB = NB // D
C4 = NB // P
HALF = P // 2
HB = HALF // D
NPAIR = 4
NSEL = 4
STEPS = J + 1
M1, M2 = 4, 2


def rows_of(j):
    return min(SH, NSHIFT - SH * j) * F


def build(nc, ids, tables, w0a, w0b, w1t, wt1, wt1d, wt2, wt3, b1, b2, dense_t, consts, out):
    f32, bf16, i32 = mybir.dt.float32, mybir.dt.bfloat16, mybir.dt.int32
    ALU, ACT = mybir.AluOpType, mybir.ActivationFunctionType
    with ExitStack() as ctx:
        def sb(name, shape, dt=f32):
            return ctx.enter_context(nc.sbuf_tensor(name, shape, dt))

        def pb(name, shape, dt=f32):
            return ctx.enter_context(nc.psum_tensor(name, shape, dt))

        def sem(name):
            return ctx.enter_context(nc.semaphore(name))

        idx = sb("idx", [P, 2, F], i32)
        rows = sb("rows", [P, 2, F, D])
        rest = sb("rest", [P, D, F])
        parts = sb("parts", [P, D, PARTS, F], bf16)
        xT = sb("xT", [R, 2, P, D], bf16)
        a_sb = sb("a_sb", [R, 2, NB])
        pairs = sb("pairs", [R, NPAIR, NB])
        h_sb = sb("h_sb", [H, NB])
        hT = sb("hT", [P, C4, H])
        xd = sb("xd", [P, 2, C4, HB, F1])
        g_sb = sb("g_sb", [H, F1, GB])
        w0x = sb("w0x", [R, 2, J, H])
        w0 = sb("w0", [R, J, H])
        w1 = sb("w1", [H, F, H])
        wt1_sb = sb("wt1_sb", [P, 2, M1 * P])
        wt1d_sb = sb("wt1d_sb", [D, M1 * P])
        wt2_sb = sb("wt2_sb", [P, M1, M2 * P])
        wt3_sb = sb("wt3_sb", [P, M2])
        b1_sb = sb("b1_sb", [P, M1])
        b2_sb = sb("b2_sb", [P, M2])
        dn = sb("dn", [D, GB])
        z = sb("z", [H, 2, GB])
        u1 = sb("u1", [P, M1, GB])
        u2 = sb("u2", [P, M2, GB])
        y = sb("y", [1, GB])
        NSELC = STEPS * R
        OX, OI, OM = NSELC, NSELC + F, NSELC + F + P
        cst = sb("cst", [P, OM + HB * F1])
        cb = sb("cb", [P, OI + P], bf16)
        select = cb[0:R, 0:NSELC].rearrange("k (u m) -> k u m", u=STEPS)
        unpart = cb[0:R, OX:OX + F]
        ident16 = cb[:, OI:OI + P]
        ident = cst[:, OI:OI + P]
        own = cst[:, OM:OM + HB * F1].rearrange("p (b f) -> p b f", b=HB)

        psel = pb("psel", [P, NSEL, NB])
        ph = pb("ph", [H, NB])
        pg = pb("pg", [H, 2, NB])
        pm = pb("pm", [P, NB])
        pm16 = pm[0:R, :].bitcast(bf16).rearrange("r (d b) -> r d b", b=P)

        s_ids = [sem("s_ids0"), sem("s_ids1")]
        s_gather = [sem("s_gather0"), sem("s_gather1")]
        s_const, s_w0, s_w1, s_mlpw = sem("s_const"), sem("s_w0"), sem("s_w1"), sem("s_mlpw")
        s_start = sem("s_start")
        s_setup = sem("s_setup")
        s_split = sem("s_split")
        s_tr, s_xT = sem("s_tr"), sem("s_xT")
        s_sel, s_a = sem("s_sel"), sem("s_a")
        s_pairs, s_main = sem("s_pairs"), sem("s_main")
        s_h, s_hTp, s_hT = sem("s_h"), sem("s_hTp"), sem("s_hT")
        s_xp, s_xd = sem("s_xp"), sem("s_xd")
        s_g, s_ga, s_gv = sem("s_g"), sem("s_ga"), sem("s_gv")
        s_z2, s_z1c, s_z2c = sem("s_z2"), sem("s_z1c"), sem("s_z2c")
        s_mlp, s_act = sem("s_mlp"), sem("s_act")
        s_dn, s_out = sem("s_dn"), sem("s_out")

        block = ctx.enter_context(nc.Block())

        @block.sync
        def _(sp):
            def load_ids(t, p):
                sp.dma_start(idx[:, p, :], ids[t, :, :]).then_inc(s_ids[p], 16)

            load_ids(0, 0)
            load_ids(1, 1)
            sp.dma_start(cst[:, :], consts[:, :]).then_inc(s_const, 16)
            sp.dma_start(w0x[:, 0, :, :], w0a[:, :, :]).then_inc(s_w0, 16)
            sp.dma_start(w0x[:, 1, :, :], w0b[:, :, :]).then_inc(s_w0, 16)
            sp.dma_start(w1[:, :, :], w1t[:, :, :]).then_inc(s_w1, 16)
            sp.dma_start(wt1_sb[:, :, :], wt1[:, :, :]).then_inc(s_mlpw, 16)
            sp.dma_start(wt1d_sb[:, :], wt1d[:, :]).then_inc(s_mlpw, 16)
            sp.dma_start(wt2_sb[:, :, :], wt2[:, :, :]).then_inc(s_mlpw, 16)
            sp.dma_start(wt3_sb[:, :], wt3[:, :]).then_inc(s_mlpw, 16)
            sp.dma_start(b1_sb[:, :], b1[:, :]).then_inc(s_mlpw, 16)
            sp.dma_start(b2_sb[:, :], b2[:, :]).then_inc(s_mlpw, 16)
            sp.dma_start(dn[:, :], dense_t[0, :, :]).then_inc(s_dn, 16)

            with sp.Fori(1, GROUPS) as g:
                for p in range(2):
                    sp.wait_ge(s_gather[p], 16 * F * g)
                    load_ids(2 * g + p, p)

        @block.gpsimd
        def _(pool):
            def gather(g, p, again):
                pool.wait_ge(s_ids[p], 16 * g + 16)
                if again:
                    pool.wait_ge(s_split, 8 * g - 8 + 4 * p + 4)
                pool.sem_inc(s_start, 1)
                for f in range(F):
                    pool.indirect_dma_start(rows[:, p, f, :], None, tables[f][:, :],
                                            bass.IndirectOffsetOnAxis(ap=idx[:, p, f:f + 1], axis=0)
                                            ).then_inc(s_gather[p], 16)

            gather(0, 0, False)
            gather(0, 1, False)
            with pool.Fori(1, GROUPS) as g:
                gather(g, 0, True)
                gather(g, 1, True)

        @block.tensor
        def _(pe):
            def transposes(t, p, half):
                pe.wait_ge(s_split, 4 * t + 4)
                for e in range(D // 2):
                    last = nc.tensor.transpose(pm16[:, e, :], parts[:, half * (D // 2) + e, :, :]
                                               .rearrange("b a f -> b (a f)"), ident16)
                last.then_inc(s_tr, 1)

            def selection(k, c, u):
                cols = xT[:, c // BPT, (c % BPT) * BB:(c % BPT + 1) * BB, :].rearrange("r b d -> r (b d)")
                m = rows_of(u - 1) if u else R
                nc.tensor.matmul(psel[0:m, u % NSEL, :], select[:, u, 0:m], cols,
                                 start=True, stop=True).then_inc(s_sel, 1)

            def free_bank(k, u, first):
                v = u - NSEL
                if v < 0:
                    if first:
                        return
                    v, k = v + STEPS, k - 1
                if v == 0:
                    pe.wait_ge(s_a, k + 1)
                else:
                    pe.wait_ge(s_pairs, J * k + v)

            def fields(k, c):
                for g in range(C4):
                    b0 = (c % BPT) * BB + g * (P // D)
                    cols = xT[:, c // BPT, b0:b0 + P // D, :].rearrange("r b d -> r (b d)")
                    last = nc.tensor.matmul(pm[:, g * F:(g + 1) * F], cols, unpart, start=True, stop=True)
                last.then_inc(s_xp, 1)

            def transpose_h(k):
                pe.wait_ge(s_h, k + 1)
                for g in range(C4):
                    last = nc.tensor.transpose(pm[:, g * P:(g + 1) * P], h_sb[:, g * P:(g + 1) * P], ident)
                last.then_inc(s_hTp, 1)

            def contract(k, c, rnd, first):
                pe.wait_ge(s_hT, k + 1)
                pe.wait_ge(s_xd, k + 1)
                if not (first and rnd == 0):
                    pe.wait_ge(s_ga, 2 * k + rnd)
                    pe.wait_ge(s_gv, 2 * k + rnd)
                for e in range(2):
                    g = 2 * rnd + e
                    for r in range(2):
                        s = slice(r * HALF, (r + 1) * HALF)
                        last = nc.tensor.matmul(pg[:, r, e * HB * F1:(e + 1) * HB * F1], hT[s, g, :],
                                                xd[s, c % 2, g, :, :].rearrange("p b f -> p (b f)"),
                                                start=True, stop=True)
                last.then_inc(s_g, 1)

            def cin2(g):
                pe.wait_ge(s_ga, 2 * CB * g + 2 * CB)
                pe.wait_ge(s_gv, 2 * CB * g + 2 * CB)
                for f in range(F):
                    last = nc.tensor.matmul(pm[:, 0:GB], w1[:, f, :], g_sb[:, f, :], start=f == 0, stop=f == F - 1)
                last.then_inc(s_z2, 1)

            def mlp(g, part):
                if part < 2:
                    if part == 0:
                        pe.wait_ge(s_z1c, g + 1)
                        pe.wait_ge(s_z2c, g + 1)
                        pe.wait_ge(s_dn, 16 * g + 16)
                    for e in range(2):
                        m = slice((2 * part + e) * P, (2 * part + e + 1) * P)
                        o = pm[:, e * GB:(e + 1) * GB]
                        nc.tensor.matmul(o, wt1_sb[:, 0, m], z[:, 0, :], start=True, stop=False)
                        nc.tensor.matmul(o, wt1_sb[:, 1, m], z[:, 1, :], start=False, stop=False)
                        last = nc.tensor.matmul(o, wt1d_sb[:, m], dn[:, :], start=False, stop=True)
                elif part == 2:
                    pe.wait_ge(s_act, 4 * g + 2)
                    for e in range(M2):
                        for a in range(M1):
                            last = nc.tensor.matmul(pm[:, e * GB:(e + 1) * GB], wt2_sb[:, a, e * P:(e + 1) * P],
                                                    u1[:, a, :], start=a == 0, stop=a == M1 - 1)
                else:
                    pe.wait_ge(s_act, 4 * g + 3)
                    for a in range(M2):
                        last = nc.tensor.matmul(pm[0:1, 0:GB], wt3_sb[:, a:a + 1], u2[:, a, :],
                                                start=a == 0, stop=a == M2 - 1)
                last.then_inc(s_mlp, 1)

            MLP_AT = {1: 0, 2: 1, 4: 2, 5: 3}

            def group(i, first, final):
                for c in range(CB):
                    k = CB * i + c
                    k0 = first and c == 0
                    for j in range(J):
                        for u in (range(j + 3, j + 4) if j < J - 1 else range(j + 3, j + 5)):
                            kk, cc, v = (k, c, u) if u < STEPS else (k + 1, c + 1, u - STEPS)
                            if final and cc == CB:
                                continue
                            if v == 0 and cc % BPT == 0:
                                pe.wait_ge(s_xT, 4 * i + 2 * (cc // BPT) + 2)
                            free_bank(kk, v, first and cc == 0)
                            selection(kk, cc % CB, v)
                        pe.wait_ge(s_pairs, J * k + j + 1)
                        if j == 0 and not k0:
                            pe.wait_ge(s_h, k)
                        m = rows_of(j)
                        nc.tensor.matmul(ph[:, :], w0[0:m, j, :], pairs[0:m, (J * c + j) % NPAIR, :],
                                         start=j == 0, stop=j == J - 1).then_inc(s_main, 1)
                        if j == 0 and not k0:
                            pe.wait_ge(s_xd, k)
                            if c == 1 and not first:
                                pe.wait_ge(s_z2c, i)
                            transpose_h(k - 1)
                        if c % BPT == BPT - 1 and not (final and c == CB - 1):
                            t = 2 * i + c // BPT + 1
                            if j == 1:
                                pe.wait_ge(s_hT, k)
                                transposes(t, (c // BPT + 1) % 2, 0)
                            if j == 3:
                                pe.wait_ge(s_xT, 2 * t + 1)
                                transposes(t, (c // BPT + 1) % 2, 1)
                        if j == 2 and not k0:
                            contract(k - 1, (c - 1) % CB, 0, first and c == 1)
                        if j == 4 and not first and c in MLP_AT:
                            pe.wait_ge(s_hT, k)
                            mlp(i - 1, MLP_AT[c])
                    if c % BPT == BPT - 1 and not (final and c == CB - 1):
                        pe.wait_ge(s_xT, 2 * (2 * i + c // BPT + 1) + 2)
                    elif not first and c in MLP_AT:
                        pe.wait_ge(s_act, 4 * (i - 1) + MLP_AT[c] + 1)
                    elif not k0:
                        pe.wait_ge(s_hT, k)
                    fields(k, c)
                    if not k0:
                        contract(k - 1, (c - 1) % CB, 1, False)
                    if c == 0 and not first:
                        pe.wait_ge(s_xd, k + 1)
                        cin2(i - 1)

            pe.wait_ge(s_setup, 1)
            transposes(0, 0, 0)
            pe.wait_ge(s_xT, 1)
            transposes(0, 0, 1)
            pe.wait_ge(s_xT, 2)
            for u in range(3):
                selection(0, 0, u)
            pe.wait_ge(s_setup, 2)
            group(0, True, False)
            pe.wait_ge(s_w1, 16)
            pe.wait_ge(s_mlpw, 16 * 6)
            with pe.Fori(1, GROUPS - 1) as i:
                group(i, False, False)
            group(GROUPS - 1, False, True)
            k = CB * GROUPS - 1
            pe.wait_ge(s_xd, k + 1)
            transpose_h(k)
            contract(k, CB - 1, 0, False)
            contract(k, CB - 1, 1, False)
            cin2(GROUPS - 1)
            pe.wait_ge(s_z2c, GROUPS)
            for part in range(4):
                if part:
                    pe.wait_ge(s_act, 4 * (GROUPS - 1) + part)
                mlp(GROUPS - 1, part)

        def g_views(c, rnd, r):
            src = pg[:, r, 0:2 * HB * F1].rearrange("q (e b f) -> q e b f", e=2, b=HB)
            b0 = c * BB + rnd * 2 * (P // D)
            dst = g_sb[:, :, b0:b0 + 2 * (P // D)].rearrange("q f (e r b) -> q r e b f", e=2, r=2)[:, r]
            return dst, src

        @block.scalar
        def _(act):
            def copy(o, i):
                return nc.scalar.activation(o, i, ACT.Copy)

            def copy_xT(t, p, half):
                act.wait_ge(s_tr, 2 * t + half + 1)
                copy(xT[:, p, :, half * (D // 2):(half + 1) * (D // 2)], pm16.rearrange("r d b -> r b d")
                     ).then_inc(s_xT, 1)

            def copy_a(k, c, early):
                act.wait_ge(s_sel, STEPS * k + 1)
                if not early:
                    act.wait_ge(s_pairs, J * (k - 1))
                copy(a_sb[:, c % 2, :], psel[0:R, 0, :]).then_inc(s_a, 1)

            def copy_h(k, k0):
                act.wait_ge(s_main, J * k + J)
                if not k0:
                    act.wait_ge(s_hTp, k)
                copy(h_sb[:, :], ph[:, :]).then_inc(s_h, 1)

            def copy_hT(k, k0):
                act.wait_ge(s_hTp, k + 1)
                if not k0:
                    act.wait_ge(s_g, 2 * k)
                copy(hT[:, :, :], pm[:, :].rearrange("p (g q) -> p g q", g=C4)).then_inc(s_hT, 1)

            def copy_g0(k, c, rnd, group):
                act.wait_ge(s_g, 2 * k + rnd + 1)
                if c == 0 and rnd == 0 and group is not None:
                    act.wait_ge(s_z1c, group)
                    act.wait_ge(s_z2, group)
                dst, src = g_views(c, rnd, 0)
                copy(dst, src).then_inc(s_ga, 1)

            def copy_z(g):
                act.wait_ge(s_gv, 2 * CB * g + 2 * CB)
                act.wait_ge(s_ga, 2 * CB * g + 2 * CB)
                copy(z[:, 0, :], g_sb[:, F, :]).then_inc(s_z1c, 1)
                act.wait_ge(s_z2, g + 1)
                copy(z[:, 1, :], pm[:, 0:GB]).then_inc(s_z2c, 1)

            def mlp_out(g, part, last_group):
                act.wait_ge(s_mlp, 4 * g + part + 1)
                if part < 2:
                    for e in range(2):
                        m = 2 * part + e
                        last = nc.scalar.activation(u1[:, m, :], pm[:, e * GB:(e + 1) * GB], ACT.Relu,
                                                    bias=b1_sb[:, m:m + 1])
                elif part == 2:
                    for e in range(2):
                        last = nc.scalar.activation(u2[:, e, :], pm[:, e * GB:(e + 1) * GB], ACT.Relu,
                                                    bias=b2_sb[:, e:e + 1])
                else:
                    last = copy(y[:, :], pm[0:1, 0:GB])
                last.then_inc(s_act, 1)
                if part == 1 and not last_group:
                    act.dma_start(dn[:, :], dense_t[g + 1, :, :]).then_inc(s_dn, 16)
                if part == 3:
                    act.wait_ge(s_act, 4 * g + 4)
                    act.dma_start(out[bass.ts(g, GB), :].rearrange("b a -> a b"), y[:, :]).then_inc(s_out, 16)

            MLP_AT = {1: 0, 2: 1, 4: 2, 5: 3}

            def group(i, first, final):
                for c in range(CB):
                    k = CB * i + c
                    k0 = first and c == 0
                    if not k0:
                        copy_hT(k - 1, first and c == 1)
                    fetch = c % BPT == BPT - 1 and not (final and c == CB - 1)
                    if fetch:
                        copy_xT(2 * i + c // BPT + 1, (c // BPT + 1) % 2, 0)
                    if not k0:
                        copy_g0(k - 1, (c - 1) % CB, 0, None if first else i)
                    if fetch:
                        copy_xT(2 * i + c // BPT + 1, (c // BPT + 1) % 2, 1)
                    if not first and c in MLP_AT:
                        mlp_out(i - 1, MLP_AT[c], False)
                    if not first and c == CB - 1:
                        act.wait_ge(s_out, 16 * i)
                    if not (final and c == CB - 1):
                        copy_a(k + 1, c + 1, k0)
                    copy_h(k, k0)
                    if not k0:
                        copy_g0(k - 1, (c - 1) % CB, 1, None)
                    if c == 0 and not first:
                        copy_z(i - 1)

            copy_xT(0, 0, 0)
            copy_xT(0, 0, 1)
            copy_a(0, 0, True)
            group(0, True, False)
            act.wait_ge(s_mlpw, 16 * 6)
            with act.Fori(1, GROUPS - 1) as i:
                group(i, False, False)
            group(GROUPS - 1, False, True)
            k = CB * GROUPS - 1
            copy_hT(k, False)
            copy_g0(k, CB - 1, 0, None)
            copy_g0(k, CB - 1, 1, None)
            copy_z(GROUPS - 1)
            for part in range(4):
                mlp_out(GROUPS - 1, part, True)
            act.wait_ge(s_out, 16 * GROUPS)

        @block.vector
        def _(dve):
            def split(t, g, p, step, again):
                x = rows[:, p, :, :].rearrange("b f d -> b d f")
                if step == 0:
                    dve.wait_ge(s_gather[p], 16 * F * g + 16 * F)
                    if again:
                        dve.wait_ge(s_tr, 2 * t)
                    ins = nc.vector.tensor_copy(parts[:, :, 0, :], x)
                else:
                    dve.wait_ge(s_split, 4 * t + step)
                    if step == 1:
                        ins = nc.vector.tensor_tensor(rest[:, :, :], x, parts[:, :, 0, :], ALU.subtract)
                    elif step == 2:
                        ins = nc.vector.tensor_copy(parts[:, :, 1, :], rest[:, :, :])
                    else:
                        ins = nc.vector.tensor_tensor(parts[:, :, 2, :], rest[:, :, :], parts[:, :, 1, :], ALU.subtract)
                ins.then_inc(s_split, 1)

            def pair(k, c, j, early):
                m = rows_of(j)
                if j == 0:
                    dve.wait_ge(s_a, k + 1)
                dve.wait_ge(s_sel, STEPS * k + j + 2)
                if not (early and j < NPAIR):
                    dve.wait_ge(s_main, J * k + j + 1 - NPAIR)
                nc.vector.tensor_tensor(pairs[0:m, (J * c + j) % NPAIR, :], a_sb[0:m, c % 2, :],
                                        psel[0:m, (j + 1) % NSEL, :], ALU.mult).then_inc(s_pairs, 1)

            def diagonal(k, c, early):
                dve.wait_ge(s_xp, k + 1)
                if not early:
                    dve.wait_ge(s_g, 2 * k - 2)
                x = pm[:, 0:C4 * F].rearrange("p (g f) -> p g f", g=C4).unsqueeze(2).to_broadcast([P, C4, HB, F])
                o = own[:, :, 0:F].unsqueeze(1).to_broadcast([P, C4, HB, F])
                nc.vector.tensor_tensor(xd[:, c % 2, :, :, 0:F], x, o, ALU.mult).then_inc(s_xd, 1)

            def copy_g1(k, c, rnd, group):
                dve.wait_ge(s_g, 2 * k + rnd + 1)
                if c == 0 and rnd == 0 and group is not None:
                    dve.wait_ge(s_z1c, group)
                    dve.wait_ge(s_z2, group)
                dst, src = g_views(c, rnd, 1)
                nc.vector.tensor_copy(dst, src).then_inc(s_gv, 1)

            def group(i, first, final):
                for c in range(CB):
                    k = CB * i + c
                    k0 = first and c == 0
                    for j in range(J):
                        pair(k, c, j, k0)
                        if j == 0 and not k0:
                            diagonal(k - 1, (c - 1) % CB, first and c <= 2)
                            if not (first and c == 1):
                                copy_g1(k - 2, (c - 2) % CB, 1, None)
                        if j == 3 and not k0:
                            copy_g1(k - 1, (c - 1) % CB, 0, None if first else i)
                        if c % BPT == BPT - 2 and j in (1, 2, 4, 5) and not (final and c == CB - 2):
                            t = 2 * i + c // BPT + 1
                            split(t, i + (c // BPT), (c // BPT + 1) % 2, (1, 2, 4, 5).index(j), True)

            dve.wait_ge(s_const, 16)
            nc.vector.tensor_copy(cb[:, :], cst[:, 0:OI + P]).then_inc(s_setup, 1)
            dve.wait_ge(s_w0, 32)
            nc.vector.tensor_tensor(w0[:, :, :], w0x[:, 0, :, :], w0x[:, 1, :, :], ALU.add).then_inc(s_setup, 1)
            for p in range(2):
                nc.vector.tensor_copy(xd[:, p, :, :, :], own.unsqueeze(1).to_broadcast([P, C4, HB, F1])
                                      ).then_inc(s_setup, 1)
            dve.wait_ge(s_setup, 4)
            for step in range(4):
                split(0, 0, 0, step, False)
            group(0, True, False)
            with dve.Fori(1, GROUPS - 1) as i:
                group(i, False, False)
            group(GROUPS - 1, False, True)
            k = CB * GROUPS - 1
            diagonal(k, CB - 1, False)
            copy_g1(k - 1, CB - 2, 1, None)
            copy_g1(k, CB - 1, 0, None)
            copy_g1(k, CB - 1, 1, None)


def constants():
    import numpy as np
    select = np.zeros((P, STEPS, R), np.float32)
    for u in range(STEPS):
        for s in range(SH):
            shift = 0 if u == 0 else SH * (u - 1) + s
            for f in range(F):
                for a in range(PARTS):
                    select[a * F + (f + shift) % F, u, s * F + f] = 1.0
    unpart = np.zeros((P, F), np.float32)
    for a in range(PARTS):
        unpart[a * F + np.arange(F), np.arange(F)] = 1.0
    own = np.zeros((P, HB, F1), np.float32)
    for p in range(P):
        own[p, (p % HALF) // D, :] = 1.0
    return np.ascontiguousarray(np.concatenate(
        [select.reshape(P, -1), unpart, np.eye(P, dtype=np.float32), own.reshape(P, -1)], axis=1))


def kernel(**inputs):
    import numpy as np
    import concourse.bacc as bacc
    from concourse.bass_utils import run_bass_kernel_spmd

    x = {n: np.asarray(a) for n, a in inputs.items()}
    w0 = x["L0_rec_W0"][:, :, 0].reshape(H, F, F)
    w0a = np.zeros((R, J, H), np.float32)
    w0b = np.zeros((R, J, H), np.float32)
    fs = np.arange(F)
    for shift in range(NSHIFT):
        j, s = divmod(shift, SH)
        q = (fs + shift) % F
        w0a[s * F:(s + 1) * F, j, :] = w0[:, fs, q].T
        if shift:
            w0b[s * F:(s + 1) * F, j, :] = w0[:, q, fs].T
    arrays = {
        "ids": np.ascontiguousarray(x["ids"].reshape(TILES, P, F)),
        **{f"tbl_{f}": np.ascontiguousarray(x[f"tbl_{f}"]) for f in range(F)},
        "w0a": w0a, "w0b": w0b,
        "w1t": np.ascontiguousarray(x["L0_rec_W1"][:, :, 0].reshape(H, F, H).transpose(2, 1, 0)),
        "wt1": np.ascontiguousarray(x["W_top1"][0:2 * H].reshape(2, P, M1 * P).transpose(1, 0, 2)),
        "wt1d": np.ascontiguousarray(x["W_top1"][2 * H:]),
        "wt2": np.ascontiguousarray(x["W_top2"].reshape(M1, P, M2 * P).transpose(1, 0, 2)),
        "wt3": np.ascontiguousarray(x["W_top3"].reshape(M2, P).T),
        "b1": np.ascontiguousarray(x["b_top1"].reshape(M1, P).T),
        "b2": np.ascontiguousarray(x["b_top2"].reshape(M2, P).T),
        "dense_t": np.ascontiguousarray(x["dense_ctx"].reshape(GROUPS, GB, D).transpose(0, 2, 1)),
        "consts": constants(),
    }
    nc = bacc.Bacc("TRN2", target_bir_lowering=False, num_devices=1)
    ap = {n: nc.dram_tensor(n, a.shape, mybir.dt.from_np(a.dtype), kind="ExternalInput").ap() for n, a in arrays.items()}
    out = nc.dram_tensor("out", (B, 1), mybir.dt.float32, kind="ExternalOutput").ap()
    build(nc, ap["ids"], [ap[f"tbl_{f}"] for f in range(F)], ap["w0a"], ap["w0b"], ap["w1t"], ap["wt1"], ap["wt1d"],
          ap["wt2"], ap["wt3"], ap["b1"], ap["b2"], ap["dense_t"], ap["consts"], out)
    result = run_bass_kernel_spmd(nc, [arrays], core_ids=[0])
    return result.results[0]["out"]
```

```python
import concourse.bass as bass
from concourse import mybir
from contextlib import ExitStack

B, F, D = 2048, 39, 16
H = 128
P = 128
F1 = F + 1
PARTS = 3
SH = 3
R = SH * F
NSHIFT = (F + 1) // 2
J = -(-NSHIFT // SH)
TILES = B // P
NB = 512
BPT = P * D // NB
CB = 2 * BPT
GB = 2 * P
GROUPS = B // GB
BB = NB // D
C4 = NB // P
HALF = P // 2
HB = HALF // D
NPAIR = 8
SPLIT = (0, 2, 4, 6)
NS = len(SPLIT)
NPART = 4
NSEL = 4
STEPS = J + 1
AHEAD = 5
M1, M2 = 4, 2


MLP_AT = {1: 0, 3: 1, 4: 2, 5: 3}


def t_parity(c):
    return (c // BPT + 1) % 2


def part_buffer(c, j):
    return (NS * c + SPLIT.index(j)) % NPART


def part_before(j):
    back, r = divmod(SPLIT.index(j) - NPART, NS)
    return back, SPLIT[r]


def rows_of(j):
    return min(SH, NSHIFT - SH * j) * F


def build(nc, ids, tables, w0a, w0b, w1t, wt1, wt1d, wt2, wt3, b1, b2, dense_t, consts, out):
    f32, f32r, bf16, i32 = mybir.dt.float32, mybir.dt.float32r, mybir.dt.bfloat16, mybir.dt.int32
    ALU, ACT = mybir.AluOpType, mybir.ActivationFunctionType
    with ExitStack() as ctx:
        def sb(name, shape, dt=f32):
            return ctx.enter_context(nc.sbuf_tensor(name, shape, dt))

        def pb(name, shape, dt=f32):
            return ctx.enter_context(nc.psum_tensor(name, shape, dt))

        def sem(name):
            return ctx.enter_context(nc.semaphore(name))

        idx = sb("idx", [P, 2, F], i32)
        rows = sb("rows", [P, 2, F, D])
        rest = sb("rest", [P, D, F])
        parts = sb("parts", [P, D, PARTS, F], bf16)
        xT = sb("xT", [R, 2, P, D], bf16)
        a_sb = sb("a_sb", [R, 2, NB])
        pairs = sb("pairs", [R, NPAIR, NB])
        pairs_hi = sb("pairs_hi", [R, NPART, NB], f32r)
        pairs_lo = sb("pairs_lo", [R, NPART, NB], f32r)
        h_sb = sb("h_sb", [H, NB])
        hT = sb("hT", [P, C4, H])
        xd = sb("xd", [P, 2, C4, HB, F1])
        g_sb = sb("g_sb", [H, F1, GB])
        w0x = sb("w0x", [R, 2, J, H])
        w0 = sb("w0", [R, J, H])
        w0_hi = sb("w0_hi", [R, J, H], f32r)
        w0_lo = sb("w0_lo", [R, J, H], f32r)
        w1 = sb("w1", [H, F, H])
        wt1_sb = sb("wt1_sb", [P, 2, M1 * P])
        wt1d_sb = sb("wt1d_sb", [D, M1 * P])
        wt2_sb = sb("wt2_sb", [P, M1, M2 * P])
        wt3_sb = sb("wt3_sb", [P, M2])
        b1_sb = sb("b1_sb", [P, M1])
        b2_sb = sb("b2_sb", [P, M2])
        dn = sb("dn", [D, GB])
        z = sb("z", [H, 2, GB])
        u1 = sb("u1", [P, M1, GB])
        u2 = sb("u2", [P, M2, GB])
        y = sb("y", [1, GB])
        NSELC = STEPS * R
        OX, OI, OM = NSELC, NSELC + F, NSELC + F + P
        cst = sb("cst", [P, OM + HB * F1])
        cb = sb("cb", [P, OI + P], bf16)
        select = cb[0:R, 0:NSELC].rearrange("k (u m) -> k u m", u=STEPS)
        unpart = cb[0:R, OX:OX + F]
        ident16 = cb[:, OI:OI + P]
        ident = cst[:, OI:OI + P]
        own = cst[:, OM:OM + HB * F1].rearrange("p (b f) -> p b f", b=HB)

        psel = pb("psel", [P, NSEL, NB])
        ph = pb("ph", [H, NB])
        pg = pb("pg", [H, 2, NB])
        pm = pb("pm", [P, NB])
        pm16 = pm[0:R, :].bitcast(bf16).rearrange("r (d b) -> r d b", b=P)

        s_ids = [sem("s_ids0"), sem("s_ids1")]
        s_gather = [sem("s_gather0"), sem("s_gather1")]
        s_const, s_w0, s_w1, s_mlpw = sem("s_const"), sem("s_w0"), sem("s_w1"), sem("s_mlpw")
        s_start = sem("s_start")
        s_setup = sem("s_setup")
        s_split = sem("s_split")
        s_tr, s_xT = sem("s_tr"), sem("s_xT")
        s_sel, s_a = sem("s_sel"), sem("s_a")
        s_pairs, s_main = sem("s_pairs"), sem("s_main")
        s_hi, s_lo = sem("s_hi"), sem("s_lo")
        s_h, s_hTp, s_hT = sem("s_h"), sem("s_hTp"), sem("s_hT")
        s_xp, s_xd = sem("s_xp"), sem("s_xd")
        s_g, s_ga = sem("s_g"), sem("s_ga")
        s_z2, s_z1c, s_z2c = sem("s_z2"), sem("s_z1c"), sem("s_z2c")
        s_mlp, s_act = sem("s_mlp"), sem("s_act")
        s_dn, s_out = sem("s_dn"), sem("s_out")

        block = ctx.enter_context(nc.Block())

        @block.sync
        def _(sp):
            def load_ids(t, p):
                sp.dma_start(idx[:, p, :], ids[t, :, :]).then_inc(s_ids[p], 16)

            load_ids(0, 0)
            load_ids(1, 1)
            sp.dma_start(cst[:, :], consts[:, :]).then_inc(s_const, 16)
            sp.dma_start(w0x[:, 0, :, :], w0a[:, :, :]).then_inc(s_w0, 16)
            sp.dma_start(w0x[:, 1, :, :], w0b[:, :, :]).then_inc(s_w0, 16)
            sp.dma_start(w1[:, :, :], w1t[:, :, :]).then_inc(s_w1, 16)
            sp.dma_start(wt1_sb[:, :, :], wt1[:, :, :]).then_inc(s_mlpw, 16)
            sp.dma_start(wt1d_sb[:, :], wt1d[:, :]).then_inc(s_mlpw, 16)
            sp.dma_start(wt2_sb[:, :, :], wt2[:, :, :]).then_inc(s_mlpw, 16)
            sp.dma_start(wt3_sb[:, :], wt3[:, :]).then_inc(s_mlpw, 16)
            sp.dma_start(b1_sb[:, :], b1[:, :]).then_inc(s_mlpw, 16)
            sp.dma_start(b2_sb[:, :], b2[:, :]).then_inc(s_mlpw, 16)
            sp.dma_start(dn[:, :], dense_t[0, :, :]).then_inc(s_dn, 16)

            with sp.Fori(1, GROUPS) as g:
                for p in range(2):
                    sp.wait_ge(s_gather[p], 16 * F * g)
                    load_ids(2 * g + p, p)

        @block.gpsimd
        def _(pool):
            def gather(g, p, again):
                pool.wait_ge(s_ids[p], 16 * g + 16)
                if again:
                    pool.wait_ge(s_split, 8 * g - 8 + 4 * p + 4)
                pool.sem_inc(s_start, 1)
                for f in range(F):
                    pool.indirect_dma_start(rows[:, p, f, :], None, tables[f][:, :],
                                            bass.IndirectOffsetOnAxis(ap=idx[:, p, f:f + 1], axis=0)
                                            ).then_inc(s_gather[p], 16)

            gather(0, 0, False)
            gather(0, 1, False)
            with pool.Fori(1, GROUPS) as g:
                gather(g, 0, True)
                gather(g, 1, True)

        @block.tensor
        def _(pe):
            def transposes(t, p, half):
                pe.wait_ge(s_split, 4 * t + 4)
                for e in range(D // 2):
                    last = nc.tensor.transpose(pm16[:, e, :], parts[:, half * (D // 2) + e, :, :]
                                               .rearrange("b a f -> b (a f)"), ident16)
                last.then_inc(s_tr, 1)

            def selection(k, c, u):
                cols = xT[:, c // BPT, (c % BPT) * BB:(c % BPT + 1) * BB, :].rearrange("r b d -> r (b d)")
                m = rows_of(u - 1) if u else R
                nc.tensor.matmul(psel[0:m, u % NSEL, :], select[:, u, 0:m], cols,
                                 start=True, stop=True).then_inc(s_sel, 1)

            def free_bank(k, u, first):
                v = u - NSEL
                if v < 0:
                    if first:
                        return
                    v, k = v + STEPS, k - 1
                if v == 0:
                    pe.wait_ge(s_a, k + 1)
                else:
                    pe.wait_ge(s_pairs, J * k + v)

            def select_step(i, c, u, first, final):
                over, v = divmod(u, STEPS)
                kk, cc = CB * i + c + over, c + over
                if final and cc == CB:
                    return
                if v == 0 and cc % BPT == 0:
                    pe.wait_ge(s_xT, 4 * i + 2 * (cc // BPT) + 2)
                free_bank(kk, v, first and cc == 0)
                selection(kk, cc % CB, v)

            def fields(k, c):
                for g in range(C4):
                    b0 = (c % BPT) * BB + g * (P // D)
                    cols = xT[:, c // BPT, b0:b0 + P // D, :].rearrange("r b d -> r (b d)")
                    last = nc.tensor.matmul(pm[:, g * F:(g + 1) * F], cols, unpart, start=True, stop=True)
                last.then_inc(s_xp, 1)

            def transpose_h(k):
                pe.wait_ge(s_h, k + 1)
                for g in range(C4):
                    last = nc.tensor.transpose(pm[:, g * P:(g + 1) * P], h_sb[:, g * P:(g + 1) * P], ident)
                last.then_inc(s_hTp, 1)

            def contract(k, c, rnd, first):
                pe.wait_ge(s_hT, k + 1)
                pe.wait_ge(s_xd, k + 1)
                if not (first and rnd == 0):
                    pe.wait_ge(s_ga, 2 * k + rnd)
                for e in range(2):
                    g = 2 * rnd + e
                    for r in range(2):
                        s = slice(r * HALF, (r + 1) * HALF)
                        last = nc.tensor.matmul(pg[:, r, e * HB * F1:(e + 1) * HB * F1], hT[s, g, :],
                                                xd[s, c % 2, g, :, :].rearrange("p b f -> p (b f)"),
                                                start=True, stop=True)
                last.then_inc(s_g, 1)

            def cin2(g):
                pe.wait_ge(s_ga, 2 * CB * g + 2 * CB)
                for f in range(F):
                    last = nc.tensor.matmul(pm[:, 0:GB], w1[:, f, :], g_sb[:, f, :], start=f == 0, stop=f == F - 1)
                last.then_inc(s_z2, 1)

            def mlp(g, part):
                if part < 2:
                    if part == 0:
                        pe.wait_ge(s_z1c, g + 1)
                        pe.wait_ge(s_z2c, g + 1)
                        pe.wait_ge(s_dn, 16 * g + 16)
                    for e in range(2):
                        m = slice((2 * part + e) * P, (2 * part + e + 1) * P)
                        o = pm[:, e * GB:(e + 1) * GB]
                        nc.tensor.matmul(o, wt1_sb[:, 0, m], z[:, 0, :], start=True, stop=False)
                        nc.tensor.matmul(o, wt1_sb[:, 1, m], z[:, 1, :], start=False, stop=False)
                        last = nc.tensor.matmul(o, wt1d_sb[:, m], dn[:, :], start=False, stop=True)
                elif part == 2:
                    pe.wait_ge(s_act, 4 * g + 2)
                    for e in range(M2):
                        for a in range(M1):
                            last = nc.tensor.matmul(pm[:, e * GB:(e + 1) * GB], wt2_sb[:, a, e * P:(e + 1) * P],
                                                    u1[:, a, :], start=a == 0, stop=a == M1 - 1)
                else:
                    pe.wait_ge(s_act, 4 * g + 3)
                    for a in range(M2):
                        last = nc.tensor.matmul(pm[0:1, 0:GB], wt3_sb[:, a:a + 1], u2[:, a, :],
                                                start=a == 0, stop=a == M2 - 1)
                last.then_inc(s_mlp, 1)

            def group(i, first, final):
                for c in range(CB):
                    k = CB * i + c
                    k0 = first and c == 0
                    fetch = c % BPT == BPT - 2 and not (final and c == CB - 2)
                    t = 2 * i + c // BPT + 1
                    for j in range(J):
                        select_step(i, c, j + AHEAD, first, final)
                        if j in SPLIT:
                            pe.wait_ge(s_lo, NS * k + SPLIT.index(j) + 1)
                        else:
                            pe.wait_ge(s_pairs, J * k + j + 1)
                        if j == 0 and not k0:
                            pe.wait_ge(s_h, k)
                        m, start, stop = rows_of(j), j == 0, j == J - 1
                        if j in SPLIT:
                            n = part_buffer(c, j)
                            hi, lo = pairs_hi[0:m, n, :], pairs_lo[0:m, n, :]
                            nc.tensor.matmul(ph[:, :], w0_hi[0:m, j, :], hi, start=start, stop=False)
                            nc.tensor.matmul(ph[:, :], w0_lo[0:m, j, :], hi, start=False, stop=False)
                            last = nc.tensor.matmul(ph[:, :], w0_hi[0:m, j, :], lo, start=False, stop=stop)
                        else:
                            last = nc.tensor.matmul(ph[:, :], w0[0:m, j, :], pairs[0:m, (J * c + j) % NPAIR, :],
                                                    start=start, stop=stop)
                        last.then_inc(s_main, 1)
                        if j == 0 and c == 1 and not first:
                            pe.wait_ge(s_z2c, i)
                            fields(k - 1, 0)
                        if j == 1 and not k0:
                            pe.wait_ge(s_xd, k)
                            transpose_h(k - 1)
                        if j == 3 and not k0:
                            contract(k - 1, (c - 1) % CB, 0, first and c == 1)
                        if j == 5 and c == 0 and not first:
                            contract(k - 1, CB - 1, 1, False)
                        if j == 3 and fetch:
                            pe.wait_ge(s_hT, k)
                            transposes(t, t_parity(c), 0)
                        if j == 5 and fetch:
                            pe.wait_ge(s_xT, 2 * t + 1)
                            transposes(t, t_parity(c), 1)
                        if j == 5 and not first and c in MLP_AT:
                            pe.wait_ge(s_hT, k)
                            mlp(i - 1, MLP_AT[c])
                    if c == 0 and not first:
                        select_step(i, c, J + AHEAD, first, final)
                        pe.wait_ge(s_hT, k)
                        cin2(i - 1)
                    else:
                        if not k0:
                            contract(k - 1, (c - 1) % CB, 1, False)
                        if fetch:
                            pe.wait_ge(s_xT, 2 * t + 2)
                        elif not first and c in MLP_AT:
                            pe.wait_ge(s_act, 4 * (i - 1) + MLP_AT[c] + 1)
                        elif not k0:
                            pe.wait_ge(s_hT, k)
                        fields(k, c)
                        select_step(i, c, J + AHEAD, first, final)

            pe.wait_ge(s_setup, 1)
            transposes(0, 0, 0)
            pe.wait_ge(s_xT, 1)
            transposes(0, 0, 1)
            pe.wait_ge(s_xT, 2)
            for u in range(AHEAD):
                free_bank(0, u, True)
                selection(0, 0, u)
            pe.wait_ge(s_setup, 4)
            group(0, True, False)
            pe.wait_ge(s_w1, 16)
            pe.wait_ge(s_mlpw, 16 * 6)
            with pe.Fori(1, GROUPS - 1) as i:
                group(i, False, False)
            group(GROUPS - 1, False, True)
            k = CB * GROUPS - 1
            pe.wait_ge(s_xd, k + 1)
            transpose_h(k)
            contract(k, CB - 1, 0, False)
            contract(k, CB - 1, 1, False)
            cin2(GROUPS - 1)
            pe.wait_ge(s_z2c, GROUPS)
            for part in range(4):
                if part:
                    pe.wait_ge(s_act, 4 * (GROUPS - 1) + part)
                mlp(GROUPS - 1, part)

        def g_views(c, rnd, r):
            src = pg[:, r, 0:2 * HB * F1].rearrange("q (e b f) -> q e b f", e=2, b=HB)
            b0 = c * BB + rnd * 2 * (P // D)
            dst = g_sb[:, :, b0:b0 + 2 * (P // D)].rearrange("q f (e r b) -> q r e b f", e=2, r=2)[:, r]
            return dst, src

        @block.scalar
        def _(act):
            def copy(o, i):
                return nc.scalar.activation(o, i, ACT.Copy)

            def copy_xT(t, p, half):
                act.wait_ge(s_tr, 2 * t + half + 1)
                copy(xT[:, p, :, half * (D // 2):(half + 1) * (D // 2)], pm16.rearrange("r d b -> r b d")
                     ).then_inc(s_xT, 1)

            def copy_a(k, c, early):
                act.wait_ge(s_sel, STEPS * k + 1)
                if not early:
                    act.wait_ge(s_pairs, J * (k - 1))
                copy(a_sb[:, c % 2, :], psel[0:R, 0, :]).then_inc(s_a, 1)

            def high(k, c, j, first):
                if j not in SPLIT:
                    return
                m, n = rows_of(j), part_buffer(c, j)
                act.wait_ge(s_pairs, J * k + j + 1)
                back, b = part_before(j)
                if not (first and c + back < 0):
                    act.wait_ge(s_main, J * (k + back) + b + 1)
                copy(pairs_hi[0:m, n, :], pairs[0:m, (J * c + j) % NPAIR, :]).then_inc(s_hi, 1)

            def copy_h(k, k0):
                act.wait_ge(s_main, J * k + J)
                if not k0:
                    act.wait_ge(s_hTp, k)
                copy(h_sb[:, :], ph[:, :]).then_inc(s_h, 1)

            def copy_hT(k, k0):
                act.wait_ge(s_hTp, k + 1)
                if not k0:
                    act.wait_ge(s_g, 2 * k)
                copy(hT[:, :, :], pm[:, :].rearrange("p (g q) -> p g q", g=C4)).then_inc(s_hT, 1)

            def copy_g(k, c, rnd, group):
                act.wait_ge(s_g, 2 * k + rnd + 1)
                if c == 0 and rnd == 0 and group is not None:
                    act.wait_ge(s_z1c, group)
                    act.wait_ge(s_z2, group)
                for r in range(2):
                    last = copy(*g_views(c, rnd, r))
                last.then_inc(s_ga, 1)

            def copy_z(g):
                act.wait_ge(s_ga, 2 * CB * g + 2 * CB)
                copy(z[:, 0, :], g_sb[:, F, :]).then_inc(s_z1c, 1)
                act.wait_ge(s_z2, g + 1)
                copy(z[:, 1, :], pm[:, 0:GB]).then_inc(s_z2c, 1)

            def mlp_out(g, part, last_group):
                act.wait_ge(s_mlp, 4 * g + part + 1)
                if part < 2:
                    for e in range(2):
                        m = 2 * part + e
                        last = nc.scalar.activation(u1[:, m, :], pm[:, e * GB:(e + 1) * GB], ACT.Relu,
                                                    bias=b1_sb[:, m:m + 1])
                elif part == 2:
                    for e in range(2):
                        last = nc.scalar.activation(u2[:, e, :], pm[:, e * GB:(e + 1) * GB], ACT.Relu,
                                                    bias=b2_sb[:, e:e + 1])
                else:
                    last = copy(y[:, :], pm[0:1, 0:GB])
                last.then_inc(s_act, 1)
                if part == 1 and not last_group:
                    act.dma_start(dn[:, :], dense_t[g + 1, :, :]).then_inc(s_dn, 16)
                if part == 3:
                    act.wait_ge(s_act, 4 * g + 4)
                    act.dma_start(out[bass.ts(g, GB), :].rearrange("b a -> a b"), y[:, :]).then_inc(s_out, 16)

            def group(i, first, final):
                for c in range(CB):
                    k = CB * i + c
                    k0 = first and c == 0
                    fetch = c % BPT == BPT - 2 and not (final and c == CB - 2)
                    t = 2 * i + c // BPT + 1
                    more = not (final and c == CB - 1)
                    for j in (3, 4):
                        high(k, c, j, first)
                    if not k0:
                        copy_hT(k - 1, first and c == 1)
                    high(k, c, 5, first)
                    high(k, c, 6, first)
                    if not k0:
                        copy_g(k - 1, (c - 1) % CB, 0, None if first else i)
                    if fetch:
                        copy_xT(t, t_parity(c), 0)
                    if more:
                        copy_a(k + 1, c + 1, k0)
                        high(k + 1, (c + 1) % CB, 0, first and c < CB - 1)
                    if fetch:
                        copy_xT(t, t_parity(c), 1)
                    if not first and c in MLP_AT:
                        mlp_out(i - 1, MLP_AT[c], False)
                    if not first and c == CB - 1:
                        act.wait_ge(s_out, 16 * i)
                    if c == 0 and not first:
                        copy_g(k - 1, CB - 1, 1, None)
                    copy_h(k, k0)
                    if more:
                        high(k + 1, (c + 1) % CB, 1, first and c < CB - 1)
                        high(k + 1, (c + 1) % CB, 2, first and c < CB - 1)
                    if c == 0 and not first:
                        copy_z(i - 1)
                    elif not k0:
                        copy_g(k - 1, (c - 1) % CB, 1, None)

            copy_xT(0, 0, 0)
            copy_xT(0, 0, 1)
            copy_a(0, 0, True)
            high(0, 0, 0, True)
            high(0, 0, 1, True)
            high(0, 0, 2, True)
            group(0, True, False)
            act.wait_ge(s_mlpw, 16 * 6)
            with act.Fori(1, GROUPS - 1) as i:
                group(i, False, False)
            group(GROUPS - 1, False, True)
            k = CB * GROUPS - 1
            copy_hT(k, False)
            copy_g(k, CB - 1, 0, None)
            copy_g(k, CB - 1, 1, None)
            copy_z(GROUPS - 1)
            for part in range(4):
                mlp_out(GROUPS - 1, part, True)
            act.wait_ge(s_out, 16 * GROUPS)

        @block.vector
        def _(dve):
            def split(t, g, p, step, again):
                x = rows[:, p, :, :].rearrange("b f d -> b d f")
                if step == 0:
                    dve.wait_ge(s_gather[p], 16 * F * g + 16 * F)
                    if again:
                        dve.wait_ge(s_tr, 2 * t)
                    ins = nc.vector.tensor_copy(parts[:, :, 0, :], x)
                else:
                    dve.wait_ge(s_split, 4 * t + step)
                    if step == 1:
                        ins = nc.vector.tensor_tensor(rest[:, :, :], x, parts[:, :, 0, :], ALU.subtract)
                    elif step == 2:
                        ins = nc.vector.tensor_copy(parts[:, :, 1, :], rest[:, :, :])
                    else:
                        ins = nc.vector.tensor_tensor(parts[:, :, 2, :], rest[:, :, :], parts[:, :, 1, :], ALU.subtract)
                ins.then_inc(s_split, 1)

            def pair(k, c, j, first):
                m = rows_of(j)
                if j == 0:
                    dve.wait_ge(s_a, k + 1)
                dve.wait_ge(s_sel, STEPS * k + j + 2)
                if not (first and J * c + j < NPAIR):
                    dve.wait_ge(s_main, J * k + j + 1 - NPAIR)
                nc.vector.tensor_tensor(pairs[0:m, (J * c + j) % NPAIR, :], a_sb[0:m, c % 2, :],
                                        psel[0:m, (j + 1) % NSEL, :], ALU.mult).then_inc(s_pairs, 1)

            def low(k, c, j, first):
                if j not in SPLIT:
                    return
                m, n = rows_of(j), part_buffer(c, j)
                dve.wait_ge(s_hi, NS * k + SPLIT.index(j) + 1)
                back, b = part_before(j)
                if not (first and c + back < 0):
                    dve.wait_ge(s_main, J * (k + back) + b + 1)
                nc.vector.tensor_tensor(pairs_lo[0:m, n, :], pairs[0:m, (J * c + j) % NPAIR, :], pairs_hi[0:m, n, :].bitcast(f32),
                                        ALU.subtract).then_inc(s_lo, 1)

            def diagonal(k, c, early):
                dve.wait_ge(s_xp, k + 1)
                if not early:
                    dve.wait_ge(s_g, 2 * k - 2)
                x = pm[:, 0:C4 * F].rearrange("p (g f) -> p g f", g=C4).unsqueeze(2).to_broadcast([P, C4, HB, F])
                o = own[:, :, 0:F].unsqueeze(1).to_broadcast([P, C4, HB, F])
                nc.vector.tensor_tensor(xd[:, c % 2, :, :, 0:F], x, o, ALU.mult).then_inc(s_xd, 1)

            def group(i, first, final):
                for c in range(CB):
                    k = CB * i + c
                    k0 = first and c == 0
                    for j in range(J):
                        pair(k, c, j, first)
                        if j:
                            low(k, c, j - 1, first)
                        elif not k0:
                            low(k - 1, (c - 1) % CB, J - 1, first)
                        if j == (3 if c == 1 and not first else 2) and not k0:
                            diagonal(k - 1, (c - 1) % CB, first and c <= 2)
                        if c % BPT == BPT - 2 and j < 4 and not (final and c == CB - 2):
                            t = 2 * i + c // BPT + 1
                            split(t, i + (c // BPT), (c // BPT + 1) % 2, j, True)

            dve.wait_ge(s_const, 16)
            nc.vector.tensor_copy(cb[:, :], cst[:, 0:OI + P]).then_inc(s_setup, 1)
            dve.wait_ge(s_w0, 32)
            nc.vector.tensor_tensor(w0[:, :, :], w0x[:, 0, :, :], w0x[:, 1, :, :], ALU.add).then_inc(s_setup, 1)
            dve.wait_ge(s_setup, 2)
            nc.vector.tensor_copy(w0_hi[:, :, :], w0[:, :, :]).then_inc(s_setup, 1)
            dve.wait_ge(s_setup, 3)
            nc.vector.tensor_tensor(w0_lo[:, :, :], w0[:, :, :], w0_hi[:, :, :].bitcast(f32), ALU.subtract
                                    ).then_inc(s_setup, 1)
            for p in range(2):
                nc.vector.tensor_copy(xd[:, p, :, :, :], own.unsqueeze(1).to_broadcast([P, C4, HB, F1])
                                      ).then_inc(s_setup, 1)
            dve.wait_ge(s_setup, 6)
            for step in range(4):
                split(0, 0, 0, step, False)
            group(0, True, False)
            with dve.Fori(1, GROUPS - 1) as i:
                group(i, False, False)
            group(GROUPS - 1, False, True)
            k = CB * GROUPS - 1
            low(k, CB - 1, J - 1, False)
            diagonal(k, CB - 1, False)


def constants():
    import numpy as np
    select = np.zeros((P, STEPS, R), np.float32)
    for u in range(STEPS):
        for s in range(SH):
            shift = 0 if u == 0 else SH * (u - 1) + s
            for f in range(F):
                for a in range(PARTS):
                    select[a * F + (f + shift) % F, u, s * F + f] = 1.0
    unpart = np.zeros((P, F), np.float32)
    for a in range(PARTS):
        unpart[a * F + np.arange(F), np.arange(F)] = 1.0
    own = np.zeros((P, HB, F1), np.float32)
    for p in range(P):
        own[p, (p % HALF) // D, :] = 1.0
    return np.ascontiguousarray(np.concatenate(
        [select.reshape(P, -1), unpart, np.eye(P, dtype=np.float32), own.reshape(P, -1)], axis=1))


def kernel(**inputs):
    import numpy as np
    import concourse.bacc as bacc
    from concourse.bass_utils import run_bass_kernel_spmd

    x = {n: np.asarray(a) for n, a in inputs.items()}
    w0 = x["L0_rec_W0"][:, :, 0].reshape(H, F, F)
    w0a = np.zeros((R, J, H), np.float32)
    w0b = np.zeros((R, J, H), np.float32)
    fs = np.arange(F)
    for shift in range(NSHIFT):
        j, s = divmod(shift, SH)
        q = (fs + shift) % F
        w0a[s * F:(s + 1) * F, j, :] = w0[:, fs, q].T
        if shift:
            w0b[s * F:(s + 1) * F, j, :] = w0[:, q, fs].T
    arrays = {
        "ids": np.ascontiguousarray(x["ids"].reshape(TILES, P, F)),
        **{f"tbl_{f}": np.ascontiguousarray(x[f"tbl_{f}"]) for f in range(F)},
        "w0a": w0a, "w0b": w0b,
        "w1t": np.ascontiguousarray(x["L0_rec_W1"][:, :, 0].reshape(H, F, H).transpose(2, 1, 0)),
        "wt1": np.ascontiguousarray(x["W_top1"][0:2 * H].reshape(2, P, M1 * P).transpose(1, 0, 2)),
        "wt1d": np.ascontiguousarray(x["W_top1"][2 * H:]),
        "wt2": np.ascontiguousarray(x["W_top2"].reshape(M1, P, M2 * P).transpose(1, 0, 2)),
        "wt3": np.ascontiguousarray(x["W_top3"].reshape(M2, P).T),
        "b1": np.ascontiguousarray(x["b_top1"].reshape(M1, P).T),
        "b2": np.ascontiguousarray(x["b_top2"].reshape(M2, P).T),
        "dense_t": np.ascontiguousarray(x["dense_ctx"].reshape(GROUPS, GB, D).transpose(0, 2, 1)),
        "consts": constants(),
    }
    nc = bacc.Bacc("TRN2", target_bir_lowering=False, num_devices=1)
    ap = {n: nc.dram_tensor(n, a.shape, mybir.dt.from_np(a.dtype), kind="ExternalInput").ap() for n, a in arrays.items()}
    out = nc.dram_tensor("out", (B, 1), mybir.dt.float32, kind="ExternalOutput").ap()
    build(nc, ap["ids"], [ap[f"tbl_{f}"] for f in range(F)], ap["w0a"], ap["w0b"], ap["w1t"], ap["wt1"], ap["wt1d"],
          ap["wt2"], ap["wt3"], ap["b1"], ap["b2"], ap["dense_t"], ap["consts"], out)
    result = run_bass_kernel_spmd(nc, [arrays], core_ids=[0])
    return result.results[0]["out"]
```
